# Optimizing a Trainium2 kernel written in Bass

```python
import numpy as np
import jax
import jax.numpy as jnp

def _softmax(x, axis=-1):
    return jax.nn.softmax(x, axis=axis)

def _gelu(x):
    return jax.nn.gelu(x, approximate=True)

def _silu(x):
    return jax.nn.silu(x)

def _sigmoid(x):
    return jax.nn.sigmoid(x)

def _layernorm(x, axis=-1, eps=1e-05):
    m = jnp.mean(x, axis=axis, keepdims=True)
    v = jnp.var(x, axis=axis, keepdims=True)
    return (x - m) / jnp.sqrt(v + eps)

def _scatter_add(tgt, idx, src, axis=0):
    return tgt.at[idx].add(src)

def _segment_sum(src, seg, n):
    return jax.ops.segment_sum(src, seg, n)
kernel_name = 'mk_cond_seq_d1_seqx_r4_b5667f'

def setup_inputs(seed: int=0):
    np.random.seed(seed)
    _w = jnp.asarray

    def _rec_inputs():
        import jax
        import jax.numpy as jnp
        _rk = jax.random.key(seed)
        x = -1.528e-05 + 0.9999 * jax.random.normal(jax.random.fold_in(_rk, 1), (4, 512, 512), jnp.float32)
        _lenS = 512 - jax.random.randint(jax.random.fold_in(_rk, 7), (4,), 0, max(1, 512 // 4) + 1, jnp.int32)
        _lenS2 = 512 - jax.random.randint(jax.random.fold_in(_rk, 8), (4,), 0, max(1, 512 // 4) + 1, jnp.int32)
        itok_B_1_2 = jax.random.randint(jax.random.fold_in(_rk, 11), (4,), 1, 3, jnp.int32)
        return (x, itok_B_1_2)
    x, itok_B_1_2 = _rec_inputs()

    def _L0_cond_setup():
        import jax, jax.numpy as jnp
        import numpy as np
        B, S, H = (8, 512, 512)
        BN = 256
        E = 3
        LN_EPS = 1e-05
        key = jax.random.key(seed)
        ks = jax.random.split(key, 8)
        stream = jax.random.randint(ks[0], (B,), 0, E, dtype=jnp.int32)
        hidden_states = jax.random.normal(ks[1], (B, S, H), dtype=jnp.float32)
        W_down = jax.random.normal(ks[2], (E, H, BN), dtype=jnp.float32) * 0.02
        b_down = jnp.zeros((E, BN), dtype=jnp.float32)
        W_up = jax.random.normal(ks[3], (E, BN, H), dtype=jnp.float32) * 0.02
        b_up = jnp.zeros((E, H), dtype=jnp.float32)
        ln_w = jnp.ones((E, H), dtype=jnp.float32)
        ln_b = jnp.zeros((E, H), dtype=jnp.float32)
        return {'stream': stream, 'hidden_states': hidden_states, 'W_down': W_down, 'b_down': b_down, 'W_up': W_up, 'b_up': b_up, 'ln_w': ln_w, 'ln_b': ln_b}
    _L0_cond_all = _L0_cond_setup()
    _L0_cond_in = {k: v for k, v in _L0_cond_all.items() if k in ('W_down', 'b_down', 'W_up', 'b_up', 'ln_w', 'ln_b')}
    del _L0_cond_all
    return {'x': x, 'itok_B_1_2': itok_B_1_2, 'L0_cond_W_down': _L0_cond_in['W_down'], 'L0_cond_b_down': _L0_cond_in['b_down'], 'L0_cond_W_up': _L0_cond_in['W_up'], 'L0_cond_b_up': _L0_cond_in['b_up'], 'L0_cond_ln_w': _L0_cond_in['ln_w'], 'L0_cond_ln_b': _L0_cond_in['ln_b']}

def reference(x, itok_B_1_2, L0_cond_W_down, L0_cond_b_down, L0_cond_W_up, L0_cond_b_up, L0_cond_ln_w, L0_cond_ln_b):
    import jax
    import jax.numpy as jnp

    def _L0_cond_ref(stream, hidden_states, W_down, b_down, W_up, b_up, ln_w, ln_b):
        import jax, jax.numpy as jnp
        import numpy as np
        B, S, H = (8, 512, 512)
        BN = 256
        E = 3
        LN_EPS = 1e-05
        Wd = W_down[stream]
        bd = b_down[stream]
        Wu = W_up[stream]
        bu = b_up[stream]
        g = ln_w[stream]
        b = ln_b[stream]
        residual = hidden_states
        h = jnp.einsum('bsh,bhk->bsk', hidden_states, Wd) + bd[:, None, :]
        h = jax.nn.gelu(h, approximate=False)
        h = jnp.einsum('bsk,bkh->bsh', h, Wu) + bu[:, None, :]
        h = residual + h
        mean = jnp.mean(h, axis=-1, keepdims=True)
        var = jnp.mean(jnp.square(h - mean), axis=-1, keepdims=True)
        h = (h - mean) * jax.lax.rsqrt(var + LN_EPS)
        return h * g[:, None, :] + b[:, None, :]
    x = _L0_cond_ref(itok_B_1_2, x, L0_cond_W_down, L0_cond_b_down, L0_cond_W_up, L0_cond_b_up, L0_cond_ln_w, L0_cond_ln_b)
    return x

_drawn_inputs = setup_inputs


def setup_inputs(seed=0):
    import zlib

    import numpy as np

    out = dict(_drawn_inputs(seed))
    spreads = {'L0_cond_b_down': (0.0, 0.416),
     'L0_cond_b_up': (0.0, 0.1),
     'L0_cond_ln_w': (1.0, 0.2),
     'L0_cond_ln_b': (0.0, 0.1)}
    factors = {}
    for name, (base, spread) in spreads.items():
        noise = np.random.default_rng([zlib.crc32(name.encode()), seed]).standard_normal(out[name].shape)
        drawn = base * np.exp(spread * noise) if base else spread * noise
        out[name] = jnp.asarray(drawn.astype(out[name].dtype))
    for name, factor in factors.items():
        out[name] = (out[name] * factor).astype(out[name].dtype)
    return out
```

```python
from contextlib import ExitStack

import concourse.bass as bass
from concourse import mybir

F32 = mybir.dt.float32
F32R = mybir.dt.float32r
ACT = mybir.ActivationFunctionType
ALU = mybir.AluOpType

P = 128
EPS = 1e-5


def conditional_adapter_kernel(
    nc: bass.Bass,
    x_cols: bass.AP,
    expert_of_batch: bass.AP,
    weights: bass.AP,
    ln_rows: bass.AP,
    out: bass.AP,
):
    B, _, KT, S = x_cols.shape
    H = KT * P
    BN = (weights.shape[2] - KT) // (2 * KT * P + 1) * P
    JT = BN // P
    TT = S // P
    WD0 = JT + KT
    WU0 = WD0 + KT * BN
    WROW = WU0 + JT * H
    HALF = KT // 2
    assert WROW == weights.shape[2]

    out_rows = out.rearrange("b (p t) h -> b p t h", t=TT)

    with ExitStack() as ctx:
        def sb(name, shape, dt=F32):
            return ctx.enter_context(nc.sbuf_tensor(name, shape, dt))

        def sem(name):
            return ctx.enter_context(nc.semaphore(name))

        def pair(name):
            return [sem(f"{name}{p}") for p in range(2)]

        x_raw = sb("x_raw", [P, 2, KT, S])
        x_res = sb("x_res", [P, 2, KT, S])
        x_hi = sb("x_hi", [P, 2, KT, S], F32R)
        x_lo = sb("x_lo", [P, 2, KT, S], F32R)
        w_raw = sb("w_raw", [P, 2, WROW])
        wd_hi = sb("wd_hi", [P, 2, KT, BN], F32R)
        wd_lo = sb("wd_lo", [P, 2, KT, BN], F32R)
        wu_hi = sb("wu_hi", [P, 2, JT, H], F32R)
        wu_lo = sb("wu_lo", [P, 2, JT, H], F32R)
        hid = sb("hid", [P, 2, JT, S])
        hid_hi = sb("hid_hi", [P, 2, JT, S], F32R)
        hid_lo = sb("hid_lo", [P, 2, JT, S], F32R)
        ln_gb = sb("ln_gb", [P, 2, 2, H])
        centred = sb("centred", [P, 2, H])
        result = sb("result", [P, 2, TT, H])
        stats = sb("stats", [P, 2, TT, 6])
        mean_var = sb("mean_var", [P, 2, TT, 2])
        var_eps = sb("var_eps", [P, 2, TT])
        rstd = sb("rstd", [P, 2, TT])
        minus_half = sb("minus_half", [P, 1])
        ident = sb("ident", [P, P])

        hid_ps = ctx.enter_context(nc.psum_tensor("hid_ps", [P, 2, JT, S], F32))
        y_ps = ctx.enter_context(nc.psum_tensor("y_ps", [P, TT, H], F32))

        def raw_wd(p, k0, k1):
            return w_raw[:, p, WD0 + k0 * BN:WD0 + k1 * BN].rearrange("q (k n) -> q k n", n=BN)

        def raw_wu(p, j0, j1):
            return w_raw[:, p, WU0 + j0 * H:WU0 + j1 * H].rearrange("q (j n) -> q j n", n=H)

        x_in = [[sem(f"x_in{p}{k}") for k in range(KT)] for p in range(2)]
        wd_in = [[sem(f"wd_in{p}{c}") for c in range(2)] for p in range(2)]
        wu_in = pair("wu_in")
        ln_in = pair("ln_in")
        ident_zero = sem("ident_zero")
        ident_done = sem("ident_done")
        half_done = sem("half_done")
        x_hi_done = pair("x_hi_done")
        x_lo_done = pair("x_lo_done")
        x_res_done = pair("x_res_done")
        wd_hi_done = pair("wd_hi_done")
        wd_lo_done = pair("wd_lo_done")
        wu_hi_done = pair("wu_hi_done")
        wu_lo_done = pair("wu_lo_done")
        hid_ps_done = pair("hid_ps_done")
        hid_done = pair("hid_done")
        hid_hi_done = pair("hid_hi_done")
        hid_lo_done = pair("hid_lo_done")
        res_placed = pair("res_placed")
        y_done = pair("y_done")
        stats_done = pair("stats_done")
        mean_done = pair("mean_done")
        var_done = pair("var_done")
        rstd_done = pair("rstd_done")
        y_free = [sem(f"y_free{t}") for t in range(TT)]
        norm_done = pair("norm_done")
        stored = pair("stored")

        block = ctx.enter_context(nc.Block())

        @block.sync
        def _(sp):
            def load_x(b):
                i, p = b // 2, b % 2
                for k in range(KT):
                    if i:
                        sp.wait_ge(x_hi_done[p], KT * (i - 1) + k + 1)
                        sp.wait_ge(x_lo_done[p], KT * (i - 1) + k + 1)
                        sp.wait_ge(x_res_done[p], KT * (i - 1) + k + 1)
                    sp.dma_start(x_raw[:, p, k, :], x_cols[b, :, k, :]).then_inc(x_in[p][k], 16)

            def load_w(b, e):
                i, p = b // 2, b % 2
                if i:
                    sp.wait_ge(wd_hi_done[p], 2 * i)
                    sp.wait_ge(wd_lo_done[p], 2 * i)
                    sp.wait_ge(hid_hi_done[p], JT * i)
                row = weights[bass.ds(e, 1), :, :].rearrange("e q n -> (e q) n")
                mid = WD0 + HALF * BN
                sp.dma_start(w_raw[:, p, 0:mid], row[:, 0:mid]).then_inc(wd_in[p][0], 16)
                sp.dma_start(w_raw[:, p, mid:WU0], row[:, mid:WU0]).then_inc(wd_in[p][1], 16)
                if i:
                    sp.wait_ge(wu_hi_done[p], JT * i)
                    sp.wait_ge(wu_lo_done[p], JT * i)
                sp.dma_start(w_raw[:, p, WU0:WROW], row[:, WU0:WROW]).then_inc(wu_in[p], 16)

            def load_ln(b, e):
                i, p = b // 2, b % 2
                if i:
                    sp.wait_ge(norm_done[p], TT * i)
                sp.dma_start(ln_gb[:, p, :, :].rearrange("q a h -> q (a h)"),
                             ln_rows[bass.ds(e, 1), :].to_broadcast([P, 2 * H])).then_inc(ln_in[p], 16)

            def store(b):
                i, p = b // 2, b % 2
                for t in range(0, TT, 2):
                    sp.wait_ge(norm_done[p], TT * i + t + 2)
                    sp.dma_start(out_rows[b, :, t:t + 2, :], result[:, p, t:t + 2, :]).then_inc(stored[p], 16)

            load_x(0)
            expert = [sp.value_load(expert_of_batch[0:1, b:b + 1], min_val=0, max_val=weights.shape[0] - 1)
                      for b in range(B)]
            load_w(0, expert[0])
            load_ln(0, expert[0])
            load_x(1)
            load_w(1, expert[1])
            load_ln(1, expert[1])
            load_x(2)
            load_w(2, expert[2])
            store(0)
            load_ln(2, expert[2])
            load_x(3)
            load_w(3, expert[3])
            store(1)
            load_ln(3, expert[3])
            store(2)
            store(3)
            for p in range(2):
                sp.wait_ge(stored[p], 16 * TT // 2 * (B // 2))

        @block.gpsimd
        def _(pool):
            nc.gpsimd.memset(ident[:], 0.0).then_inc(ident_zero, 1)
            nc.gpsimd.memset(minus_half[:], -0.5).then_inc(half_done, 1)
            pool.wait_ge(ident_zero, 1)
            nc.gpsimd.affine_select(out=ident[:], in_=ident[:], compare_op=ALU.not_equal, fill=1.0, base=0,
                                    pattern=[[-1, P]], channel_multiplier=1).then_inc(ident_done, 1)
            pool.wait_ge(half_done, 1)

            def split_lo(b):
                i, p = b // 2, b % 2
                for k in range(KT):
                    pool.wait_ge(x_hi_done[p], KT * i + k + 1)
                    if i and k == 0:
                        pool.wait_ge(hid_ps_done[p], JT * i)
                    nc.gpsimd.tensor_tensor(x_lo[:, p, k, :], x_raw[:, p, k, :], x_hi[:, p, k, :].bitcast(F32),
                                            ALU.subtract).then_inc(x_lo_done[p], 1)
                    if k % 2 == 0:
                        c = k // 2
                        pool.wait_ge(wd_hi_done[p], 2 * i + c + 1)
                        nc.gpsimd.tensor_tensor(wd_lo[:, p, 2 * c:2 * c + 2, :], raw_wd(p, 2 * c, 2 * c + 2),
                                                wd_hi[:, p, 2 * c:2 * c + 2, :].bitcast(F32),
                                                ALU.subtract).then_inc(wd_lo_done[p], 1)
                for j in range(JT):
                    pool.wait_ge(wu_hi_done[p], JT * i + j + 1)
                    if i and j == 0:
                        pool.wait_ge(y_done[p], TT * i)
                    nc.gpsimd.tensor_tensor(wu_lo[:, p, j, :], raw_wu(p, j, j + 1)[:, 0, :],
                                            wu_hi[:, p, j, :].bitcast(F32), ALU.subtract).then_inc(wu_lo_done[p], 1)

            def inverse_std(b):
                i, p = b // 2, b % 2
                for t in range(TT):
                    pool.wait_ge(var_done[p], TT * i + t + 1)
                    nc.gpsimd.tensor_tensor(rstd[:, p, t:t + 1], var_eps[:, p, t:t + 1], minus_half[:],
                                            ALU.pow).then_inc(rstd_done[p], 1)

            split_lo(0)
            for b in range(B):
                if b + 1 < B:
                    split_lo(b + 1)
                inverse_std(b)

        @block.scalar
        def _(act):
            def split_x(b):
                i, p = b // 2, b % 2
                for k in range(KT):
                    act.wait_ge(x_in[p][k], 16 * (i + 1))
                    if i and k == 0:
                        act.wait_ge(hid_ps_done[p], JT * i)
                    nc.scalar.activation(x_hi[:, p, k, :], x_raw[:, p, k, :], ACT.Copy).then_inc(x_hi_done[p], 1)
                    if k % 2 == 0:
                        c = k // 2
                        act.wait_ge(wd_in[p][c], 16 * (i + 1))
                        nc.scalar.activation(wd_hi[:, p, 2 * c:2 * c + 2, :], raw_wd(p, 2 * c, 2 * c + 2),
                                             ACT.Copy).then_inc(wd_hi_done[p], 1)

            def split_wu(b):
                i, p = b // 2, b % 2
                act.wait_ge(wu_in[p], 16 * (i + 1))
                if i:
                    act.wait_ge(y_done[p], TT * i)
                for j in range(JT):
                    nc.scalar.activation(wu_hi[:, p, j, :], raw_wu(p, j, j + 1)[:, 0, :],
                                         ACT.Copy).then_inc(wu_hi_done[p], 1)

            def gelu(b):
                i, p = b // 2, b % 2
                for j in range(JT):
                    act.wait_ge(hid_ps_done[p], JT * i + j + 1)
                    nc.scalar.activation(hid[:, p, j, :], hid_ps[:, p, j, :], ACT.Gelu,
                                         bias=w_raw[:, p, j:j + 1]).then_inc(hid_done[p], 1)
                    nc.scalar.activation(hid_hi[:, p, j, :], hid_ps[:, p, j, :], ACT.Gelu,
                                         bias=w_raw[:, p, j:j + 1]).then_inc(hid_hi_done[p], 1)

            split_x(0)
            split_wu(0)
            for b in range(B):
                if b + 1 < B:
                    split_x(b + 1)
                gelu(b)
                if b + 1 < B:
                    split_wu(b + 1)

        @block.vector
        def _(dve):
            def residual(b):
                i, p = b // 2, b % 2
                dve.wait_ge(wd_in[p][0], 16 * (i + 1))
                if i:
                    dve.wait_ge(res_placed[p], i)
                for k in range(KT):
                    dve.wait_ge(x_in[p][k], 16 * (i + 1))
                    nc.vector.tensor_scalar(x_res[:, p, k, :], x_raw[:, p, k, :], w_raw[:, p, JT + k:JT + k + 1],
                                            None, ALU.add).then_inc(x_res_done[p], 1)

            def split_hidden(b):
                i, p = b // 2, b % 2
                for j in range(JT):
                    dve.wait_ge(hid_done[p], JT * i + j + 1)
                    dve.wait_ge(hid_hi_done[p], JT * i + j + 1)
                    nc.vector.tensor_tensor(hid_lo[:, p, j, :], hid[:, p, j, :], hid_hi[:, p, j, :].bitcast(F32),
                                            ALU.subtract).then_inc(hid_lo_done[p], 1)

            def layer_norm(b):
                i, p = b // 2, b % 2

                def scale(t):
                    n = TT * i + t + 1
                    dve.wait_ge(rstd_done[p], n)
                    nc.vector.scalar_tensor_tensor(out=result[:, p, t, :], in0=centred[:, t % 2, :],
                                                   scalar=rstd[:, p, t:t + 1], in1=ln_gb[:, p, 1, :],
                                                   op0=ALU.mult, op1=ALU.add).then_inc(norm_done[p], 1)

                dve.wait_ge(ln_in[p], 16 * (i + 1))
                if i:
                    dve.wait_ge(stored[p], 16 * (TT // 2) * i)
                for t in range(TT):
                    n = TT * i + t + 1
                    dve.wait_ge(y_done[p], n)
                    nc.vector.bn_stats(stats[:, p, t, :], y_ps[:, t, :]).then_inc(stats_done[p], 1)
                    dve.wait_ge(stats_done[p], n)
                    nc.vector.bn_aggr(mean_var[:, p, t, :], stats[:, p, t, :]).then_inc(mean_done[p], 1)
                    dve.wait_ge(mean_done[p], n)
                    nc.vector.tensor_scalar(var_eps[:, p, t:t + 1], mean_var[:, p, t, 1:2], EPS, None,
                                            ALU.add).then_inc(var_done[p], 1)
                    nc.vector.scalar_tensor_tensor(out=centred[:, t % 2, :], in0=y_ps[:, t, :],
                                                   scalar=mean_var[:, p, t, 0:1], in1=ln_gb[:, p, 0, :],
                                                   op0=ALU.subtract, op1=ALU.mult).then_inc(y_free[t], 1)
                    dve.wait_ge(y_free[t], b + 1)
                    if t >= 1:
                        scale(t - 1)
                scale(TT - 1)

            residual(0)
            for b in range(B):
                split_hidden(b)
                if b + 1 < B:
                    residual(b + 1)
                layer_norm(b)

        @block.tensor
        def _(pe):
            def down(b):
                i, p = b // 2, b % 2
                for j in range(JT):
                    cols = slice(j * P, (j + 1) * P)
                    for k in range(KT):
                        if j == 0:
                            if k % 2 == 0:
                                pe.wait_ge(wd_hi_done[p], 2 * i + k // 2 + 1)
                            pe.wait_ge(x_hi_done[p], KT * i + k + 1)
                        nc.tensor.matmul(hid_ps[:, p, j, :], wd_hi[:, p, k, cols], x_hi[:, p, k, :],
                                         start=(k == 0), stop=False)
                        if j == 0:
                            pe.wait_ge(x_lo_done[p], KT * i + k + 1)
                        nc.tensor.matmul(hid_ps[:, p, j, :], wd_hi[:, p, k, cols], x_lo[:, p, k, :],
                                         start=False, stop=False)
                        if j == 0 and k % 2 == 0:
                            pe.wait_ge(wd_lo_done[p], 2 * i + k // 2 + 1)
                        last = nc.tensor.matmul(hid_ps[:, p, j, :], wd_lo[:, p, k, cols], x_hi[:, p, k, :],
                                                start=False, stop=(k == KT - 1))
                    last.then_inc(hid_ps_done[p], 1)

            def place_residual(b):
                i, p = b // 2, b % 2
                pe.wait_ge(x_res_done[p], KT * (i + 1))
                for t in range(TT):
                    if b:
                        pe.wait_ge(y_free[t], b)
                    for k in range(KT):
                        last = nc.tensor.matmul(y_ps[:, t, k * P:(k + 1) * P], x_res[:, p, k, t * P:(t + 1) * P],
                                                ident[:], start=(k == 0), stop=False, is_transpose=True,
                                                skip_group_check=True)
                last.then_inc(res_placed[p], 1)

            def up(b):
                i, p = b // 2, b % 2
                for j in range(JT):
                    pe.wait_ge(hid_hi_done[p], JT * i + j + 1)
                    pe.wait_ge(wu_hi_done[p], JT * i + j + 1)
                    pe.wait_ge(wu_lo_done[p], JT * i + j + 1)
                    for t in range(TT):
                        rows = slice(t * P, (t + 1) * P)
                        nc.tensor.matmul(y_ps[:, t, :], hid_hi[:, p, j, rows], wu_hi[:, p, j, :],
                                         start=False, stop=False, skip_group_check=True)
                        nc.tensor.matmul(y_ps[:, t, :], hid_hi[:, p, j, rows], wu_lo[:, p, j, :],
                                         start=False, stop=False, skip_group_check=True)
                        if t == 0:
                            pe.wait_ge(hid_lo_done[p], JT * i + j + 1)
                        last = nc.tensor.matmul(y_ps[:, t, :], hid_lo[:, p, j, rows], wu_hi[:, p, j, :],
                                                start=False, stop=(j == JT - 1), skip_group_check=True)
                        if j == JT - 1:
                            last.then_inc(y_done[p], 1)

            pe.wait_ge(ident_done, 1)
            for b in range(B):
                down(b)
                place_residual(b)
                up(b)


def kernel(x, itok_B_1_2, L0_cond_W_down, L0_cond_b_down, L0_cond_W_up, L0_cond_b_up, L0_cond_ln_w, L0_cond_ln_b):
    import numpy as np
    import concourse.bacc as bacc
    from concourse.bass_utils import run_bass_kernel_spmd

    x = np.asarray(x)
    B, S, H = x.shape
    E, _, BN = L0_cond_W_down.shape
    kt, jt, tt = H // P, BN // P, S // P
    by_partition = lambda a, n: np.asarray(a).reshape(E, n, P, -1).transpose(0, 2, 1, 3).reshape(E, P, -1)
    arrays = {
        "x_cols": np.ascontiguousarray(x.reshape(B, P, tt, kt, P).transpose(0, 4, 3, 2, 1).reshape(B, P, kt, S)),
        "expert_of_batch": np.ascontiguousarray(np.asarray(itok_B_1_2).reshape(1, B)),
        "weights": np.concatenate([by_partition(L0_cond_b_down, jt), by_partition(L0_cond_b_up, kt),
                                   by_partition(L0_cond_W_down, kt), by_partition(L0_cond_W_up, jt)], axis=2),
        "ln_rows": np.concatenate([np.asarray(L0_cond_ln_w), np.asarray(L0_cond_ln_b)], axis=1),
    }
    nc = bacc.Bacc("TRN2", target_bir_lowering=False, num_devices=1)
    ins = [nc.dram_tensor(name, a.shape, mybir.dt.from_np(a.dtype), kind="ExternalInput").ap()
           for name, a in arrays.items()]
    out = nc.dram_tensor("out", (B, S, H), F32, kind="ExternalOutput").ap()
    conditional_adapter_kernel(nc, *ins, out)
    r = run_bass_kernel_spmd(nc, [arrays], core_ids=[0])
    return r.results[0]["out"]
```

```python
from contextlib import ExitStack

import concourse.bass as bass
from concourse import mybir

F32 = mybir.dt.float32
F32R = mybir.dt.float32r
ACT = mybir.ActivationFunctionType
ALU = mybir.AluOpType

P = 128
EPS = 1e-5


def conditional_adapter_kernel(
    nc: bass.Bass,
    x_cols: bass.AP,
    expert_of_batch: bass.AP,
    weights: bass.AP,
    ln_rows: bass.AP,
    out: bass.AP,
):
    B, _, KT, S = x_cols.shape
    H = KT * P
    BN = (weights.shape[2] - KT) // (2 * KT * P + 1) * P
    JT = BN // P
    TT = S // P
    WD0 = JT + KT
    WU0 = WD0 + KT * BN
    WROW = WU0 + JT * H
    HALF = KT // 2
    assert WROW == weights.shape[2]

    out_rows = out.rearrange("b (p t) h -> b p t h", t=TT)

    with ExitStack() as ctx:
        def sb(name, shape, dt=F32):
            return ctx.enter_context(nc.sbuf_tensor(name, shape, dt))

        def sem(name):
            return ctx.enter_context(nc.semaphore(name))

        def pair(name):
            return [sem(f"{name}{p}") for p in range(2)]

        x_raw = sb("x_raw", [P, 2, KT, S])
        x_res = sb("x_res", [P, 2, KT, S])
        x_hi = sb("x_hi", [P, 2, KT, S], F32R)
        x_lo = sb("x_lo", [P, 2, KT, S], F32R)
        w_raw = sb("w_raw", [P, 2, WROW])
        wd_hi = sb("wd_hi", [P, 2, KT, BN], F32R)
        wd_lo = sb("wd_lo", [P, 2, KT, BN], F32R)
        wu_hi = sb("wu_hi", [P, 2, JT, H], F32R)
        wu_lo = sb("wu_lo", [P, 2, JT, H], F32R)
        hid_hi = sb("hid_hi", [P, 2, JT, S], F32R)
        hid_lo = sb("hid_lo", [P, 2, JT, S], F32R)
        ln_gb = sb("ln_gb", [P, 2, 2, H])
        result = sb("result", [P, 2, TT, H])
        stats = sb("stats", [P, 2, TT, 6])
        mean_var = sb("mean_var", [P, 2, TT, 2])
        var_eps = sb("var_eps", [P, 2, TT])
        rstd = sb("rstd", [P, 2, TT])
        minus_half = sb("minus_half", [P, TT])
        ident = sb("ident", [P, P])

        hid_ps = ctx.enter_context(nc.psum_tensor("hid_ps", [P, 2, JT, S], F32))
        y_ps = ctx.enter_context(nc.psum_tensor("y_ps", [P, TT, H], F32))

        def raw_wd(p, k0, k1):
            return w_raw[:, p, WD0 + k0 * BN:WD0 + k1 * BN].rearrange("q (k n) -> q k n", n=BN)

        def raw_wu(p, j0, j1):
            return w_raw[:, p, WU0 + j0 * H:WU0 + j1 * H].rearrange("q (j n) -> q j n", n=H)

        x_in = [[sem(f"x_in{p}{k}") for k in range(KT)] for p in range(2)]
        wd_in = [[sem(f"wd_in{p}{c}") for c in range(2)] for p in range(2)]
        wu_in = pair("wu_in")
        ln_in = pair("ln_in")
        stored = [[sem(f"stored{p}{t}") for t in range(TT)] for p in range(2)]
        ident_zero = sem("ident_zero")
        ident_done = sem("ident_done")
        half_done = sem("half_done")
        x_hi_done = sem("x_hi_done")
        x_lo_done = sem("x_lo_done")
        x_res_done = sem("x_res_done")
        wd_hi_done = sem("wd_hi_done")
        wd_lo_done = sem("wd_lo_done")
        wu_hi_done = sem("wu_hi_done")
        wu_lo_done = [sem(f"wu_lo_done{j}") for j in range(JT)]
        hid_ps_done = sem("hid_ps_done")
        hid_hi_done = sem("hid_hi_done")
        hid_done = sem("hid_done")
        hid_lo_done = sem("hid_lo_done")
        res_placed = sem("res_placed")
        y_done = sem("y_done")
        stats_done = sem("stats_done")
        mean_done = sem("mean_done")
        var_done = sem("var_done")
        rstd_done = sem("rstd_done")
        y_free = sem("y_free")
        scaled = sem("scaled")
        norm_done = sem("norm_done")
        last_norm_done = sem("last_norm_done")

        def loaded(eng, semaphore, b):
            eng.wait_ge(semaphore, 16 * (b // 2 + 1))

        block = ctx.enter_context(nc.Block())

        @block.sync
        def _(sp):
            def load_x(b, ks):
                p = b % 2
                for k in ks:
                    if b >= 2:
                        sp.wait_ge(x_res_done, KT * (b - 2) + k + 1)
                        if b == 2:
                            sp.wait_ge(hid_ps_done, JT)
                        else:
                            sp.wait_ge(x_lo_done, KT * (b - 3) + k + 1)
                    sp.dma_start(x_raw[:, p, k, :], x_cols[b, :, k, :]).then_inc(x_in[p][k], 16)

            def row_of(e):
                return weights[bass.ds(e, 1), :, :].rearrange("e q n -> (e q) n")

            def load_wd(b, e, cs):
                p = b % 2
                if b >= 2:
                    sp.wait_ge(hid_done, JT * (b - 1))
                    if b > 2:
                        sp.wait_ge(wd_lo_done, 2 * (b - 2))
                mid = WD0 + HALF * BN
                for c in cs:
                    a, z = ((0, mid), (mid, WU0))[c]
                    sp.dma_start(w_raw[:, p, a:z], row_of(e)[:, a:z]).then_inc(wd_in[p][c], 16)

            def load_wu(b, e):
                p = b % 2
                if b >= 2:
                    for j in range(JT):
                        sp.wait_ge(wu_lo_done[j], b - 1)
                sp.dma_start(w_raw[:, p, WU0:WROW], row_of(e)[:, WU0:WROW]).then_inc(wu_in[p], 16)

            def load_ln(b, e):
                p = b % 2
                if b >= 2:
                    sp.wait_ge(norm_done, TT * (b - 1))
                sp.dma_start(ln_gb[:, p, :, :].rearrange("q a h -> q (a h)"),
                             ln_rows[bass.ds(e, 1), :].to_broadcast([P, 2 * H])).then_inc(ln_in[p], 16)

            def store(b):
                p = b % 2
                for t in range(TT):
                    if TT * b + t + 1 == TT * B:
                        sp.wait_ge(last_norm_done, 1)
                    else:
                        sp.wait_ge(norm_done, TT * b + t + 1)
                    sp.dma_start(out_rows[b, :, t, :], result[:, p, t, :]).then_inc(stored[p][t], 16)

            def expert_of(b):
                return sp.value_load(expert_of_batch[0:1, b:b + 1], min_val=0, max_val=weights.shape[0] - 1)

            expert = [expert_of(0)]
            load_wd(0, expert[0], [0, 1])
            load_wu(0, expert[0])
            load_x(1, range(KT))
            expert.append(expert_of(1))
            load_wd(1, expert[1], [0, 1])
            load_wu(1, expert[1])
            load_ln(0, expert[0])
            expert.append(expert_of(2))
            expert.append(expert_of(3))
            load_x(2, range(KT))
            load_wd(2, expert[2], [0, 1])
            load_wu(2, expert[2])
            load_ln(1, expert[1])
            load_x(3, range(KT))
            load_wd(3, expert[3], [0, 1])
            store(0)
            load_ln(2, expert[2])
            load_wu(3, expert[3])
            store(1)
            load_ln(3, expert[3])
            store(2)
            store(3)
            for p in range(2):
                for t in range(TT):
                    sp.wait_ge(stored[p][t], 16 * (B // 2))

        @block.gpsimd
        def _(pool):
            def lo_x(b, k):
                pool.wait_ge(x_hi_done, 2 * (b - 1) + k // 2 + 1)
                if b > 2 and k == 0:
                    pool.wait_ge(hid_ps_done, JT * (b - 1))
                nc.gpsimd.tensor_tensor(x_lo[:, b % 2, k, :], x_raw[:, b % 2, k, :],
                                        x_hi[:, b % 2, k, :].bitcast(F32), ALU.subtract).then_inc(x_lo_done, 1)

            def lo_wd(b, c):
                pool.wait_ge(wd_hi_done, b)
                nc.gpsimd.tensor_tensor(wd_lo[:, b % 2, 2 * c:2 * c + 2, :], raw_wd(b % 2, 2 * c, 2 * c + 2),
                                        wd_hi[:, b % 2, 2 * c:2 * c + 2, :].bitcast(F32),
                                        ALU.subtract).then_inc(wd_lo_done, 1)

            def lo_wu(b, j):
                pool.wait_ge(wu_hi_done, b + 1)
                if b >= 2:
                    pool.wait_ge(y_done, TT * (b - 1))
                nc.gpsimd.tensor_tensor(wu_lo[:, b % 2, j, :], raw_wu(b % 2, j, j + 1)[:, 0, :],
                                        wu_hi[:, b % 2, j, :].bitcast(F32), ALU.subtract).then_inc(wu_lo_done[j], 1)

            def inverse_std(b, t0, t1):
                pool.wait_ge(var_done, TT * b + t1)
                nc.gpsimd.tensor_tensor(rstd[:, b % 2, t0:t1], var_eps[:, b % 2, t0:t1], minus_half[:, t0:t1],
                                        ALU.pow).then_inc(rstd_done, t1 - t0)

            def add_shift(b, t):
                p = b % 2
                pool.wait_ge(scaled, t + 1)
                nc.gpsimd.tensor_tensor(result[:, p, t, :], result[:, p, t, :], ln_gb[:, p, 1, :],
                                        ALU.add).then_inc(norm_done, 1)

            nc.gpsimd.memset(ident[:], 0.0).then_inc(ident_zero, 1)
            nc.gpsimd.memset(minus_half[:], -0.5).then_inc(half_done, 1)
            pool.wait_ge(ident_zero, 1)
            nc.gpsimd.affine_select(out=ident[:], in_=ident[:], compare_op=ALU.not_equal, fill=1.0, base=0,
                                    pattern=[[-1, P]], channel_multiplier=1).then_inc(ident_done, 1)
            pool.wait_ge(half_done, 1)
            lo_wu(0, 0)
            for b in range(B):
                if b + 1 < B:
                    lo_x(b + 1, 0)
                    lo_x(b + 1, 1)
                    lo_wd(b + 1, 0)
                if b >= 1:
                    inverse_std(b - 1, 0, TT)
                if b + 1 < B:
                    lo_wd(b + 1, 1)
                    lo_x(b + 1, 2)
                    lo_x(b + 1, 3)
                    lo_wu(b + 1, 0)
            for t in range(TT):
                inverse_std(B - 1, t, t + 1)
                if t >= 1:
                    add_shift(B - 1, t - 1)

        @block.scalar
        def _(act):
            def hi_x(b, c):
                p = b % 2
                for k in range(2 * c, 2 * c + 2):
                    loaded(act, x_in[p][k], b)
                if b > 2 and c == 0:
                    act.wait_ge(hid_ps_done, JT * (b - 1))
                nc.scalar.activation(x_hi[:, p, 2 * c:2 * c + 2, :], x_raw[:, p, 2 * c:2 * c + 2, :],
                                     ACT.Copy).then_inc(x_hi_done, 1)

            def hi_wd(b):
                p = b % 2
                for c in range(2):
                    loaded(act, wd_in[p][c], b)
                nc.scalar.activation(wd_hi[:, p, :, :], raw_wd(p, 0, KT), ACT.Copy).then_inc(wd_hi_done, 1)

            def hi_wu(b):
                p = b % 2
                loaded(act, wu_in[p], b)
                if b >= 2:
                    act.wait_ge(y_done, TT * (b - 1))
                nc.scalar.activation(wu_hi[:, p, :, :], raw_wu(p, 0, JT), ACT.Copy).then_inc(wu_hi_done, 1)

            def residual(b):
                p = b % 2
                loaded(act, wd_in[p][0], b)
                if b >= 2:
                    act.wait_ge(res_placed, b - 1)
                for k in range(KT):
                    loaded(act, x_in[p][k], b)
                    nc.scalar.activation(x_res[:, p, k, :], x_raw[:, p, k, :], ACT.Identity,
                                         bias=w_raw[:, p, JT + k:JT + k + 1]).then_inc(x_res_done, 1)

            def gelu(b, j):
                p = b % 2
                act.wait_ge(hid_ps_done, JT * b + j + 1)
                nc.scalar.activation(hid_hi[:, p, j, :], hid_ps[:, p, j, :], ACT.Gelu,
                                     bias=w_raw[:, p, j:j + 1]).then_inc(hid_hi_done, 1)
                act.wait_ge(hid_hi_done, JT * b + j + 1)
                nc.scalar.activation(hid_ps[:, p, j, :], hid_ps[:, p, j, :], ACT.Gelu,
                                     bias=w_raw[:, p, j:j + 1]).then_inc(hid_done, 1)

            def scale(b, t):
                p = b % 2
                act.wait_ge(rstd_done, TT * b + t + 1)
                act.wait_ge(y_free, TT * b + t + 1)
                nc.scalar.activation(result[:, p, t, :], result[:, p, t, :], ACT.Copy,
                                     scale=rstd[:, p, t:t + 1]).then_inc(scaled, 1)

            for k in range(KT):
                act.dma_start(x_raw[:, 0, k, :], x_cols[0, :, k, :]).then_inc(x_in[0][k], 16)
            nc.scalar.preload_act_table(ACT.Gelu)
            residual(0)
            hi_wu(0)
            for b in range(B):
                if b + 1 < B:
                    hi_x(b + 1, 0)
                    hi_wd(b + 1)
                gelu(b, 0)
                if b + 1 < B:
                    hi_x(b + 1, 1)
                gelu(b, 1)
                if b + 1 < B:
                    hi_wu(b + 1)
                    residual(b + 1)
            for t in range(TT - 1):
                scale(B - 1, t)

        @block.vector
        def _(dve):
            def lo_hidden(b, j):
                p = b % 2
                dve.wait_ge(hid_done, JT * b + j + 1)
                nc.vector.tensor_tensor(hid_lo[:, p, j, :], hid_ps[:, p, j, :], hid_hi[:, p, j, :].bitcast(F32),
                                        ALU.subtract).then_inc(hid_lo_done, 1)

            def lo_wu(b, j):
                dve.wait_ge(wu_hi_done, b + 1)
                nc.vector.tensor_tensor(wu_lo[:, b % 2, j, :], raw_wu(b % 2, j, j + 1)[:, 0, :],
                                        wu_hi[:, b % 2, j, :].bitcast(F32), ALU.subtract).then_inc(wu_lo_done[j], 1)

            def tile_stats(b, t):
                dve.wait_ge(y_done, TT * b + t + 1)
                nc.vector.bn_stats(stats[:, b % 2, t, :], y_ps[:, t, :]).then_inc(stats_done, 1)

            def moments(b, t):
                n = TT * b + t + 1
                dve.wait_ge(stats_done, n)
                nc.vector.bn_aggr(mean_var[:, b % 2, t, :], stats[:, b % 2, t, :]).then_inc(mean_done, 1)

            def centre(b, t):
                p = b % 2
                n = TT * b + t + 1
                dve.wait_ge(mean_done, n)
                nc.vector.tensor_scalar(var_eps[:, p, t:t + 1], mean_var[:, p, t, 1:2], EPS, None,
                                        ALU.add).then_inc(var_done, 1)
                if b >= 2:
                    dve.wait_ge(stored[p][t], 16 * (b // 2))
                if t == 0:
                    loaded(dve, ln_in[p], b)
                nc.vector.scalar_tensor_tensor(out=result[:, p, t, :], in0=y_ps[:, t, :],
                                               scalar=mean_var[:, p, t, 0:1], in1=ln_gb[:, p, 0, :],
                                               op0=ALU.subtract, op1=ALU.mult).then_inc(y_free, 1)

            def scale(b, t):
                p = b % 2
                n = TT * b + t + 1
                dve.wait_ge(rstd_done, n)
                dve.wait_ge(y_free, n)
                done = last_norm_done if n == B * TT else norm_done
                nc.vector.scalar_tensor_tensor(out=result[:, p, t, :], in0=result[:, p, t, :],
                                               scalar=rstd[:, p, t:t + 1], in1=ln_gb[:, p, 1, :],
                                               op0=ALU.mult, op1=ALU.add).then_inc(done, 1)

            lo_wu(0, 1)
            for j in range(JT):
                lo_hidden(0, j)
            for b in range(B):
                last = b == B - 1
                tile_stats(b, 0)
                for t in range(TT):
                    if not last and t + 1 < TT:
                        tile_stats(b, t + 1)
                    moments(b, t)
                    centre(b, t)
                    if last and t + 1 < TT:
                        tile_stats(b, t + 1)
                if last:
                    scale(b, TT - 1)
                else:
                    lo_hidden(b + 1, 0)
                    for t in range(TT):
                        scale(b, t)
                    lo_hidden(b + 1, 1)
                    lo_wu(b + 1, 1)

        @block.tensor
        def _(pe):
            def down_whole(b):
                p = b % 2
                for j in range(JT):
                    for k in range(KT):
                        if j == 0:
                            loaded(pe, x_in[p][k], b)
                            if k % 2 == 0:
                                loaded(pe, wd_in[p][k // 2], b)
                        last = nc.tensor.matmul(hid_ps[:, p, j, :], raw_wd(p, k, k + 1)[:, 0, j * P:(j + 1) * P],
                                                x_raw[:, p, k, :], start=(k == 0), stop=(k == KT - 1))
                    last.then_inc(hid_ps_done, 1)

            def down(b):
                p = b % 2
                for j in range(JT):
                    cols = slice(j * P, (j + 1) * P)
                    for k in range(KT):
                        if j == 0:
                            pe.wait_ge(wd_hi_done, b)
                            pe.wait_ge(x_hi_done, 2 * (b - 1) + k // 2 + 1)
                        nc.tensor.matmul(hid_ps[:, p, j, :], wd_hi[:, p, k, cols], x_hi[:, p, k, :],
                                         start=(k == 0), stop=False)
                        if j == 0:
                            pe.wait_ge(x_lo_done, KT * (b - 1) + k + 1)
                        nc.tensor.matmul(hid_ps[:, p, j, :], wd_hi[:, p, k, cols], x_lo[:, p, k, :],
                                         start=False, stop=False)
                        if j == 0 and k % 2 == 0:
                            pe.wait_ge(wd_lo_done, 2 * (b - 1) + k // 2 + 1)
                        last = nc.tensor.matmul(hid_ps[:, p, j, :], wd_lo[:, p, k, cols], x_hi[:, p, k, :],
                                                start=False, stop=(k == KT - 1))
                    last.then_inc(hid_ps_done, 1)

            def place_residual(b):
                p = b % 2
                pe.wait_ge(x_res_done, KT * (b + 1))
                for t in range(TT):
                    if b:
                        pe.wait_ge(y_free, TT * (b - 1) + t + 1)
                    for k in range(KT):
                        last = nc.tensor.matmul(y_ps[:, t, k * P:(k + 1) * P], x_res[:, p, k, t * P:(t + 1) * P],
                                                ident[:], start=(k == 0), stop=False, is_transpose=True,
                                                skip_group_check=True)
                last.then_inc(res_placed, 1)

            def up(b):
                p = b % 2
                for t, j in [(0, 0), (1, 0), (0, 1), (1, 1), (2, 0), (2, 1), (3, 0), (3, 1)]:
                    rows = slice(t * P, (t + 1) * P)
                    if t == 0:
                        pe.wait_ge(hid_hi_done, JT * b + j + 1)
                        pe.wait_ge(wu_hi_done, b + 1)
                        pe.wait_ge(wu_lo_done[j], b + 1)
                    nc.tensor.matmul(y_ps[:, t, :], hid_hi[:, p, j, rows], wu_hi[:, p, j, :],
                                     start=False, stop=False, skip_group_check=True)
                    nc.tensor.matmul(y_ps[:, t, :], hid_hi[:, p, j, rows], wu_lo[:, p, j, :],
                                     start=False, stop=False, skip_group_check=True)
                    if t == 0:
                        pe.wait_ge(hid_lo_done, JT * b + j + 1)
                    last = nc.tensor.matmul(y_ps[:, t, :], hid_lo[:, p, j, rows], wu_hi[:, p, j, :],
                                            start=False, stop=(j == JT - 1), skip_group_check=True)
                    if j == JT - 1:
                        last.then_inc(y_done, 1)

            for b in range(B):
                if b == 0:
                    down_whole(b)
                    pe.wait_ge(ident_done, 1)
                else:
                    down(b)
                place_residual(b)
                up(b)


def kernel(x, itok_B_1_2, L0_cond_W_down, L0_cond_b_down, L0_cond_W_up, L0_cond_b_up, L0_cond_ln_w, L0_cond_ln_b):
    import numpy as np
    import concourse.bacc as bacc
    from concourse.bass_utils import run_bass_kernel_spmd

    x = np.asarray(x)
    B, S, H = x.shape
    E, _, BN = L0_cond_W_down.shape
    kt, jt, tt = H // P, BN // P, S // P
    by_partition = lambda a, n: np.asarray(a).reshape(E, n, P, -1).transpose(0, 2, 1, 3).reshape(E, P, -1)
    arrays = {
        "x_cols": np.ascontiguousarray(x.reshape(B, P, tt, kt, P).transpose(0, 4, 3, 2, 1).reshape(B, P, kt, S)),
        "expert_of_batch": np.ascontiguousarray(np.asarray(itok_B_1_2).reshape(1, B)),
        "weights": np.concatenate([by_partition(L0_cond_b_down, jt), by_partition(L0_cond_b_up, kt),
                                   by_partition(L0_cond_W_down, kt), by_partition(L0_cond_W_up, jt)], axis=2),
        "ln_rows": np.concatenate([np.asarray(L0_cond_ln_w), np.asarray(L0_cond_ln_b)], axis=1),
    }
    nc = bacc.Bacc("TRN2", target_bir_lowering=False, num_devices=1)
    ins = [nc.dram_tensor(name, a.shape, mybir.dt.from_np(a.dtype), kind="ExternalInput").ap()
           for name, a in arrays.items()]
    out = nc.dram_tensor("out", (B, S, H), F32, kind="ExternalOutput").ap()
    conditional_adapter_kernel(nc, *ins, out)
    r = run_bass_kernel_spmd(nc, [arrays], core_ids=[0])
    return r.results[0]["out"]
```

```python
from contextlib import ExitStack

import concourse.bass as bass
from concourse import mybir

F32 = mybir.dt.float32
F32R = mybir.dt.float32r
ACT = mybir.ActivationFunctionType
ALU = mybir.AluOpType

P = 128
WARM_UP_PRODUCTS = 7
EPS = 1e-5
DMA = 16


def conditional_adapter_kernel(
    nc: bass.Bass,
    x_cols: bass.AP,
    expert_of_batch: bass.AP,
    weights: bass.AP,
    ln_rows: bass.AP,
    out: bass.AP,
):
    B, _, KT, S = x_cols.shape
    H = KT * P
    BN = (weights.shape[2] - KT) // (2 * KT * P + 1) * P
    JT = BN // P
    TT = S // P
    WD0 = JT + KT
    WU0 = WD0 + KT * BN
    WROW = WU0 + JT * H
    HALF = KT // 2
    assert WROW == weights.shape[2]
    assert (B, KT, JT, TT) == (4, 4, 2, 4) and H <= 512 and S <= 512

    out_rows = out.rearrange("b (p t) h -> b p t h", t=TT)

    with ExitStack() as ctx:
        def sb(name, shape, dt=F32):
            return ctx.enter_context(nc.sbuf_tensor(name, shape, dt))

        def sem(name):
            return ctx.enter_context(nc.semaphore(name))

        def pair(name):
            return [sem(f"{name}{p}") for p in range(2)]

        x_raw = sb("x_raw", [P, 2, KT, S])
        x_res = sb("x_res", [P, 2, KT, S])
        x_hi = sb("x_hi", [P, 2, KT, S], F32R)
        x_lo = sb("x_lo", [P, 2, KT, S], F32R)
        w_raw = sb("w_raw", [P, 2, WROW])
        wd_hi = sb("wd_hi", [P, 2, KT, BN], F32R)
        wd_lo = sb("wd_lo", [P, 2, KT, BN], F32R)
        wu_hi = sb("wu_hi", [P, 2, JT, H], F32R)
        wu_lo = sb("wu_lo", [P, 2, JT, H], F32R)
        hid_hi = sb("hid_hi", [P, 2, JT, S], F32R)
        hid_lo = sb("hid_lo", [P, 2, JT, S], F32R)
        ln_gb = sb("ln_gb", [P, 2, 2, H])
        result = sb("result", [P, 2, TT, H])
        stats = sb("stats", [P, 2, TT, 6])
        mean_var = sb("mean_var", [P, 2, TT, 2])
        var_eps = sb("var_eps", [P, 2, TT])
        rstd = sb("rstd", [P, 2, TT])
        minus_half = sb("minus_half", [P, TT])
        ident = sb("ident", [P, P])

        hid_ps = ctx.enter_context(nc.psum_tensor("hid_ps", [P, 2, JT, S], F32))
        y_ps = ctx.enter_context(nc.psum_tensor("y_ps", [P, TT, H], F32))

        def raw_wd(p, k0, k1):
            return w_raw[:, p, WD0 + k0 * BN:WD0 + k1 * BN].rearrange("q (k n) -> q k n", n=BN)

        def raw_wu(p, j0, j1):
            return w_raw[:, p, WU0 + j0 * H:WU0 + j1 * H].rearrange("q (j n) -> q j n", n=H)

        first_x_in = [sem(f"first_x_in{k}") for k in range(KT)]
        x_in = [[sem(f"x_in{p}{c}") for c in range(2)] for p in range(2)]
        first_wd_in = [sem(f"first_wd_in{c}") for c in range(2)]
        wd_in = pair("wd_in")
        wu_in = pair("wu_in")
        ln_in = pair("ln_in")
        stored = [[sem(f"stored{p}{c}") for c in range(2)] for p in range(2)]
        stored_last = [sem(f"stored_last{t}") for t in range(TT)]
        ident_zero = sem("ident_zero")
        ident_done = sem("ident_done")
        half_done = sem("half_done")
        x_hi_done = sem("x_hi_done")
        x_lo_done = sem("x_lo_done")
        x_res_done = sem("x_res_done")
        wd_hi_done = sem("wd_hi_done")
        wd_lo_done = sem("wd_lo_done")
        wu_hi_done = sem("wu_hi_done")
        wu_lo_done = [sem(f"wu_lo_done{j}") for j in range(JT)]
        first_x_hi_done = sem("first_x_hi_done")
        first_x_lo_done = sem("first_x_lo_done")
        first_wd_hi_done = sem("first_wd_hi_done")
        first_wd_lo_done = sem("first_wd_lo_done")
        hid_ps_done = sem("hid_ps_done")
        hid_hi_done = sem("hid_hi_done")
        hid_done = sem("hid_done")
        hid_lo_done = sem("hid_lo_done")
        res_placed = sem("res_placed")
        y_done = sem("y_done")
        stats_done = sem("stats_done")
        mean_done = sem("mean_done")
        var_done = sem("var_done")
        rstd_done = sem("rstd_done")
        centred = sem("centred")
        scaled = sem("scaled")
        shifted = sem("shifted")
        norm_done = sem("norm_done")
        last_norm_done = sem("last_norm_done")

        def psum_of_half(b, half):
            return b % 2 if half == 0 else 1 - b % 2

        def half_tokens(half):
            return slice(half * S // 2, (half + 1) * S // 2)

        def loaded(eng, semaphore, b):
            eng.wait_ge(semaphore, DMA * (b // 2 + 1))

        def x_loaded(eng, b, k):
            if b == 0:
                eng.wait_ge(first_x_in[k], DMA)
            else:
                eng.wait_ge(x_in[b % 2][k // HALF], DMA * ((b + 1) // 2))

        shared_tiles = [(B - 2, TT - 1)] + [(B - 1, t) for t in range(TT - 2)]

        block = ctx.enter_context(nc.Block())


        @block.sync
        def _(sp):
            def load_x(b, c):
                p = b % 2
                ks = slice(HALF * c, HALF * (c + 1))
                if b >= 2:
                    sp.wait_ge(x_res_done, KT * (b - 2) + HALF * (c + 1))
                    if b == 2:
                        sp.wait_ge(hid_ps_done, JT)
                    else:
                        sp.wait_ge(x_lo_done, KT * (b - 3) + HALF * (c + 1))
                sp.dma_start(x_raw[:, p, ks, :], x_cols[b, :, ks, :]).then_inc(x_in[p][c], DMA)

            def row_of(e):
                return weights[bass.ds(e, 1), :, :].rearrange("e q n -> (e q) n")

            def load_wd(b, e):
                p = b % 2
                if b == 0:
                    mid = WD0 + BN
                    sp.dma_start(w_raw[:, 0, 0:mid], row_of(e)[:, 0:mid]).then_inc(first_wd_in[0], DMA)
                    sp.dma_start(w_raw[:, 0, mid:WU0], row_of(e)[:, mid:WU0]).then_inc(first_wd_in[1], DMA)
                    return
                if b >= 2:
                    sp.wait_ge(hid_done, JT * (b - 1))
                    sp.wait_ge(x_res_done, KT * (b - 1))
                    if b > 2:
                        sp.wait_ge(wd_lo_done, 2 * (b - 2))
                sp.dma_start(w_raw[:, p, 0:WU0], row_of(e)[:, 0:WU0]).then_inc(wd_in[p], DMA)

            def load_wu(b, e):
                p = b % 2
                if b >= 2:
                    for j in range(JT):
                        sp.wait_ge(wu_lo_done[j], b - 1)
                sp.dma_start(w_raw[:, p, WU0:WROW], row_of(e)[:, WU0:WROW]).then_inc(wu_in[p], DMA)

            def load_ln(b, e):
                p = b % 2
                if b >= 2:
                    sp.wait_ge(norm_done, TT * (b - 1))
                sp.dma_start(ln_gb[:, p, :, :].rearrange("q a h -> q (a h)"),
                             ln_rows[bass.ds(e, 1), :].to_broadcast([P, 2 * H])).then_inc(ln_in[p], DMA)

            def store(b):
                p = b % 2
                for t in range(0, TT, 2):
                    if (b, t + 1) in shared_tiles:
                        sp.wait_ge(norm_done, TT * b + t + 1)
                        sp.wait_ge(shifted, shared_tiles.index((b, t + 1)) + 1)
                    else:
                        sp.wait_ge(norm_done, TT * b + t + 2)
                    sp.dma_start(out_rows[b, :, t:t + 2, :], result[:, p, t:t + 2, :]).then_inc(stored[p][t // 2], DMA)

            def store_last():
                b, p = B - 1, (B - 1) % 2
                for t in range(TT):
                    if t < TT - 2:
                        sp.wait_ge(shifted, shared_tiles.index((b, t)) + 1)
                    else:
                        sp.wait_ge(last_norm_done, t - TT + 3)
                    sp.dma_start(out_rows[b, :, t, :], result[:, p, t, :]).then_inc(stored_last[t], DMA)

            def expert_of(b):
                return sp.value_load(expert_of_batch[0:1, b:b + 1], min_val=0, max_val=weights.shape[0] - 1)

            expert = [expert_of(0)]
            load_wd(0, expert[0])
            for k in range(HALF, KT):
                sp.dma_start(x_raw[:, 0, k, :], x_cols[0, :, k, :]).then_inc(first_x_in[k], DMA)
            load_wu(0, expert[0])
            load_x(1, 0)
            load_x(1, 1)
            expert.append(expert_of(1))
            load_wd(1, expert[1])
            load_wu(1, expert[1])
            load_ln(0, expert[0])
            expert.append(expert_of(2))
            expert.append(expert_of(3))
            load_x(2, 0)
            load_x(2, 1)
            load_wd(2, expert[2])
            load_wu(2, expert[2])
            load_ln(1, expert[1])
            load_x(3, 0)
            load_x(3, 1)
            load_wd(3, expert[3])
            store(0)
            load_ln(2, expert[2])
            load_wu(3, expert[3])
            store(1)
            load_ln(3, expert[3])
            store(2)
            store_last()
            for c in range(2):
                sp.wait_ge(stored[0][c], DMA * (B // 2))
                sp.wait_ge(stored[1][c], DMA * (B // 2 - 1))
            for t in range(TT):
                sp.wait_ge(stored_last[t], DMA)

        @block.gpsimd
        def _(pool):
            def lo_x(b, k):
                pool.wait_ge(x_hi_done, 2 * (b - 1) + k // HALF + 1)
                if b >= 2 and k == 0:
                    pool.wait_ge(hid_ps_done, JT * (b - 1))
                nc.gpsimd.tensor_tensor(x_lo[:, b % 2, k, :], x_raw[:, b % 2, k, :],
                                        x_hi[:, b % 2, k, :].bitcast(F32), ALU.subtract).then_inc(x_lo_done, 1)

            def lo_wd(b, c):
                pool.wait_ge(wd_hi_done, b)
                p, k0, k1 = b % 2, HALF * c, HALF * (c + 1)
                nc.gpsimd.tensor_tensor(wd_lo[:, p, k0:k1, :], raw_wd(p, k0, k1),
                                        wd_hi[:, p, k0:k1, :].bitcast(F32), ALU.subtract).then_inc(wd_lo_done, 1)

            def lo_wu(b, j):
                pool.wait_ge(wu_hi_done, b + 1)
                if b >= 2:
                    pool.wait_ge(y_done, TT * (b - 1))
                nc.gpsimd.tensor_tensor(wu_lo[:, b % 2, j, :], raw_wu(b % 2, j, j + 1)[:, 0, :],
                                        wu_hi[:, b % 2, j, :].bitcast(F32), ALU.subtract).then_inc(wu_lo_done[j], 1)

            def inverse_std(b, t0, t1):
                pool.wait_ge(var_done, TT * b + t1)
                nc.gpsimd.tensor_tensor(rstd[:, b % 2, t0:t1], var_eps[:, b % 2, t0:t1], minus_half[:, t0:t1],
                                        ALU.pow).then_inc(rstd_done, t1 - t0)

            def add_shift(b, t):
                p = b % 2
                pool.wait_ge(scaled, shared_tiles.index((b, t)) + 1)
                nc.gpsimd.tensor_tensor(result[:, p, t, :], result[:, p, t, :], ln_gb[:, p, 1, :],
                                        ALU.add).then_inc(shifted, 1)

            nc.gpsimd.memset(ident[:], 0.0).then_inc(ident_zero, 1)
            nc.gpsimd.memset(minus_half[:], -0.5).then_inc(half_done, 1)
            pool.wait_ge(ident_zero, 1)
            nc.gpsimd.affine_select(out=ident[:], in_=ident[:], compare_op=ALU.not_equal, fill=1.0, base=0,
                                    pattern=[[-1, P]], channel_multiplier=1).then_inc(ident_done, 1)
            pool.wait_ge(half_done, 1)
            pool.wait_ge(first_wd_hi_done, 1)
            nc.gpsimd.tensor_tensor(wd_lo[:, 0, :, P:BN], raw_wd(0, 0, KT)[:, :, P:BN],
                                    wd_hi[:, 0, :, P:BN].bitcast(F32), ALU.subtract).then_inc(first_wd_lo_done, 1)
            lo_wu(0, 0)
            for b in range(B):
                more = b + 1 < B
                if more:
                    lo_x(b + 1, 0)
                if b:
                    inverse_std(b - 1, 0, 2)
                if more:
                    lo_x(b + 1, 1)
                    lo_wd(b + 1, 0)
                if b:
                    inverse_std(b - 1, 2, TT)
                if more:
                    lo_wd(b + 1, 1)
                    lo_x(b + 1, 2)
                    lo_x(b + 1, 3)
                    lo_wu(b + 1, 0)
            add_shift(*shared_tiles[0])
            for t in range(TT):
                inverse_std(B - 1, t, t + 1)
                if t < TT - 2:
                    add_shift(B - 1, t)

        @block.scalar
        def _(act):
            def hi_x(b, c):
                p = b % 2
                x_loaded(act, b, HALF * c)
                if b >= 2 and c == 0:
                    act.wait_ge(hid_ps_done, JT * (b - 1))
                nc.scalar.activation(x_hi[:, p, HALF * c:HALF * (c + 1), :], x_raw[:, p, HALF * c:HALF * (c + 1), :],
                                     ACT.Copy).then_inc(x_hi_done, 1)

            def wd_loaded(b):
                if b == 0:
                    act.wait_ge(first_wd_in[0], DMA)
                    act.wait_ge(first_wd_in[1], DMA)
                else:
                    act.wait_ge(wd_in[b % 2], DMA * ((b + 1) // 2))

            def hi_wd(b):
                p = b % 2
                wd_loaded(b)
                nc.scalar.activation(wd_hi[:, p, :, :], raw_wd(p, 0, KT), ACT.Copy).then_inc(wd_hi_done, 1)

            def first_hi_wd():
                wd_loaded(0)
                nc.scalar.activation(wd_hi[:, 0, :, P:BN], raw_wd(0, 0, KT)[:, :, P:BN],
                                     ACT.Copy).then_inc(first_wd_hi_done, 1)

            def hi_wu(b):
                p = b % 2
                loaded(act, wu_in[p], b)
                if b >= 2:
                    act.wait_ge(y_done, TT * (b - 1))
                nc.scalar.activation(wu_hi[:, p, :, :], raw_wu(p, 0, JT), ACT.Copy).then_inc(wu_hi_done, 1)

            def residual(b):
                p = b % 2
                wd_loaded(b)
                if b >= 2:
                    act.wait_ge(res_placed, TT * (b - 1))
                for k in range(KT):
                    x_loaded(act, b, k)
                    nc.scalar.activation(x_res[:, p, k, :], x_raw[:, p, k, :], ACT.Identity,
                                         bias=w_raw[:, p, JT + k:JT + k + 1]).then_inc(x_res_done, 1)

            def gelu(b, j):
                p = b % 2
                act.wait_ge(hid_ps_done, JT * b + j + 1)
                nc.scalar.activation(hid_hi[:, p, j, :], hid_ps[:, p, j, :], ACT.Gelu,
                                     bias=w_raw[:, p, j:j + 1]).then_inc(hid_hi_done, 1)
                nc.scalar.activation(hid_ps[:, p, j, :], hid_ps[:, p, j, :], ACT.Gelu,
                                     bias=w_raw[:, p, j:j + 1]).then_inc(hid_done, 1)

            def scale(b, t):
                p = b % 2
                act.wait_ge(rstd_done, TT * b + t + 1)
                act.wait_ge(centred, TT * b + t + 1)
                nc.scalar.activation(result[:, p, t, :], result[:, p, t, :], ACT.Copy,
                                     scale=rstd[:, p, t:t + 1]).then_inc(scaled, 1)

            def gelu_half(b, half, j):
                p = b % 2
                q = psum_of_half(b, half)
                tokens = half_tokens(half)
                act.wait_ge(hid_ps_done, JT * (b + half) + j + 1)
                nc.scalar.activation(hid_hi[:, p, j, tokens], hid_ps[:, q, j, 0:S // 2], ACT.Gelu,
                                     bias=w_raw[:, p, j:j + 1]).then_inc(hid_hi_done, 1)
                nc.scalar.activation(hid_ps[:, q, j, 0:S // 2], hid_ps[:, q, j, 0:S // 2], ACT.Gelu,
                                     bias=w_raw[:, p, j:j + 1]).then_inc(hid_done, 1)

            for k in range(HALF):
                act.dma_start(x_raw[:, 0, k, :], x_cols[0, :, k, :]).then_inc(first_x_in[k], DMA)
            nc.scalar.preload_act_table(ACT.Gelu)
            first_hi_wd()
            residual(0)
            hi_wu(0)
            for b in range(B - 1):
                hi_x(b + 1, 0)
                if b == 0:
                    gelu(b, 0)
                    gelu(b, 1)
                    hi_wd(b + 1)
                    hi_x(b + 1, 1)
                    hi_wu(b + 1)
                else:
                    hi_wd(b + 1)
                    hi_x(b + 1, 1)
                    gelu(b, 0)
                    hi_wu(b + 1)
                    gelu(b, 1)
                residual(b + 1)
            gelu_half(B - 1, 0, 0)
            gelu_half(B - 1, 0, 1)
            gelu_half(B - 1, 1, 0)
            scale(*shared_tiles[0])
            gelu_half(B - 1, 1, 1)
            for b, t in shared_tiles[1:]:
                scale(b, t)

        @block.vector
        def _(dve):
            def first_split_x():
                for k in range(KT):
                    x_loaded(dve, 0, k)
                    nc.vector.tensor_copy(x_hi[:, 0, k, :], x_raw[:, 0, k, :]).then_inc(first_x_hi_done, 1)
                    dve.wait_ge(first_x_hi_done, k + 1)
                    nc.vector.tensor_tensor(x_lo[:, 0, k, :], x_raw[:, 0, k, :], x_hi[:, 0, k, :].bitcast(F32),
                                            ALU.subtract).then_inc(first_x_lo_done, 1)

            def lo_hidden(b, j):
                p = b % 2
                dve.wait_ge(hid_done, JT * b + j + 1)
                nc.vector.tensor_tensor(hid_lo[:, p, j, :], hid_ps[:, p, j, :], hid_hi[:, p, j, :].bitcast(F32),
                                        ALU.subtract).then_inc(hid_lo_done, 1)

            def lo_hidden_half(b, half, j):
                p = b % 2
                q = psum_of_half(b, half)
                tokens = half_tokens(half)
                dve.wait_ge(hid_done, JT * (b + half) + j + 1)
                nc.vector.tensor_tensor(hid_lo[:, p, j, tokens], hid_ps[:, q, j, 0:S // 2],
                                        hid_hi[:, p, j, tokens].bitcast(F32), ALU.subtract).then_inc(hid_lo_done, 1)

            def lo_wu(b, j):
                dve.wait_ge(wu_hi_done, b + 1)
                nc.vector.tensor_tensor(wu_lo[:, b % 2, j, :], raw_wu(b % 2, j, j + 1)[:, 0, :],
                                        wu_hi[:, b % 2, j, :].bitcast(F32), ALU.subtract).then_inc(wu_lo_done[j], 1)

            def tile_stats(b, t):
                dve.wait_ge(y_done, TT * b + t + 1)
                nc.vector.bn_stats(stats[:, b % 2, t, :], y_ps[:, t, :]).then_inc(stats_done, 1)

            def moments(b, t):
                n = TT * b + t + 1
                dve.wait_ge(stats_done, n)
                nc.vector.bn_aggr(mean_var[:, b % 2, t, :], stats[:, b % 2, t, :]).then_inc(mean_done, 1)

            def shift_var(b, t0, t1):
                dve.wait_ge(mean_done, TT * b + t1)
                nc.vector.tensor_scalar(var_eps[:, b % 2, t0:t1], mean_var[:, b % 2, t0:t1, 1], EPS, None,
                                        ALU.add).then_inc(var_done, t1 - t0)

            def centre(b, t):
                p = b % 2
                n = TT * b + t + 1
                dve.wait_ge(mean_done, n)
                if b >= 2:
                    dve.wait_ge(stored[p][t // 2], DMA * (b // 2))
                if t == 0:
                    loaded(dve, ln_in[p], b)
                nc.vector.scalar_tensor_tensor(out=result[:, p, t, :], in0=y_ps[:, t, :],
                                               scalar=mean_var[:, p, t, 0:1], in1=ln_gb[:, p, 0, :],
                                               op0=ALU.subtract, op1=ALU.mult).then_inc(centred, 1)

            def scale(b, t):
                p = b % 2
                n = TT * b + t + 1
                dve.wait_ge(rstd_done, n)
                dve.wait_ge(centred, n)
                done = last_norm_done if n > B * TT - 2 else norm_done
                nc.vector.scalar_tensor_tensor(out=result[:, p, t, :], in0=result[:, p, t, :],
                                               scalar=rstd[:, p, t:t + 1], in1=ln_gb[:, p, 1, :],
                                               op0=ALU.mult, op1=ALU.add).then_inc(done, 1)

            first_split_x()
            lo_wu(0, 1)
            for j in range(JT):
                lo_hidden(0, j)
            for b in range(B - 1):
                for t in range(0, TT, 2):
                    tile_stats(b, t)
                    tile_stats(b, t + 1)
                    moments(b, t)
                    moments(b, t + 1)
                    centre(b, t)
                    shift_var(b, t, t + 2)
                    centre(b, t + 1)
                if b + 1 < B - 1:
                    scale(b, 0)
                    lo_hidden(b + 1, 0)
                    scale(b, 1)
                    lo_wu(b + 1, 1)
                    lo_hidden(b + 1, 1)
                    scale(b, 2)
                    scale(b, 3)
                else:
                    lo_wu(b + 1, 1)
                    lo_hidden_half(b + 1, 0, 0)
                    lo_hidden_half(b + 1, 0, 1)
                    scale(b, 0)
                    lo_hidden_half(b + 1, 1, 0)
                    scale(b, 1)
                    scale(b, 2)
                    tile_stats(b + 1, 0)
                    moments(b + 1, 0)
                    shift_var(b + 1, 0, 1)
                    centre(b + 1, 0)
                    lo_hidden_half(b + 1, 1, 1)
            b = B - 1
            for t in range(1, TT):
                tile_stats(b, t)
                moments(b, t)
                shift_var(b, t, t + 1)
                centre(b, t)
            scale(b, TT - 2)
            scale(b, TT - 1)

        @block.tensor
        def _(pe):
            def warm_up():
                pe.wait_ge(ident_done, 1)
                for _ in range(WARM_UP_PRODUCTS):
                    nc.tensor.matmul(y_ps[:, 0, 0:P], ident[:], ident[:], start=True, stop=True)

            def down_whole(b, j):
                for k in range(KT):
                    x_loaded(pe, b, k)
                    if k < 2:
                        pe.wait_ge(first_wd_in[k], DMA)
                    last = nc.tensor.matmul(hid_ps[:, b % 2, j, :], raw_wd(b % 2, k, k + 1)[:, 0, j * P:(j + 1) * P],
                                            x_raw[:, b % 2, k, :], start=(k == 0), stop=(k == KT - 1))
                last.then_inc(hid_ps_done, 1)

            def down(b, j):
                p = b % 2
                cols = slice(j * P, (j + 1) * P)
                for k in range(KT):
                    if b == 0:
                        pe.wait_ge(first_wd_hi_done, 1)
                        pe.wait_ge(first_x_hi_done, k + 1)
                    elif j == 0:
                        pe.wait_ge(wd_hi_done, b)
                        pe.wait_ge(x_hi_done, 2 * (b - 1) + k // HALF + 1)
                    nc.tensor.matmul(hid_ps[:, p, j, :], wd_hi[:, p, k, cols], x_hi[:, p, k, :],
                                     start=(k == 0), stop=False)
                    if b == 0:
                        pe.wait_ge(first_x_lo_done, k + 1)
                    elif j == 0:
                        pe.wait_ge(x_lo_done, KT * (b - 1) + k + 1)
                    nc.tensor.matmul(hid_ps[:, p, j, :], wd_hi[:, p, k, cols], x_lo[:, p, k, :],
                                     start=False, stop=False)
                    if b == 0:
                        pe.wait_ge(first_wd_lo_done, 1)
                    elif j == 0 and k % HALF == 0:
                        pe.wait_ge(wd_lo_done, 2 * (b - 1) + k // HALF + 1)
                    last = nc.tensor.matmul(hid_ps[:, p, j, :], wd_lo[:, p, k, cols], x_hi[:, p, k, :],
                                            start=False, stop=(k == KT - 1))
                last.then_inc(hid_ps_done, 1)

            def down_half(b, half, j):
                p = b % 2
                q = psum_of_half(b, half)
                cols = slice(j * P, (j + 1) * P)
                tokens = half_tokens(half)
                for k in range(KT):
                    if (half, j) == (0, 0):
                        pe.wait_ge(wd_hi_done, b)
                        pe.wait_ge(x_hi_done, 2 * (b - 1) + k // HALF + 1)
                    nc.tensor.matmul(hid_ps[:, q, j, 0:S // 2], wd_hi[:, p, k, cols], x_hi[:, p, k, tokens],
                                     start=(k == 0), stop=False)
                    if (half, j) == (0, 0):
                        pe.wait_ge(x_lo_done, KT * (b - 1) + k + 1)
                    nc.tensor.matmul(hid_ps[:, q, j, 0:S // 2], wd_hi[:, p, k, cols], x_lo[:, p, k, tokens],
                                     start=False, stop=False)
                    if (half, j) == (0, 0) and k % HALF == 0:
                        pe.wait_ge(wd_lo_done, 2 * (b - 1) + k // HALF + 1)
                    last = nc.tensor.matmul(hid_ps[:, q, j, 0:S // 2], wd_lo[:, p, k, cols], x_hi[:, p, k, tokens],
                                            start=False, stop=(k == KT - 1))
                last.then_inc(hid_ps_done, 1)

            def place_residual(b, t):
                if b:
                    pe.wait_ge(centred, TT * (b - 1) + t + 1)
                for k in range(KT):
                    last = nc.tensor.matmul(y_ps[:, t, k * P:(k + 1) * P], x_res[:, b % 2, k, t * P:(t + 1) * P],
                                            ident[:], start=(k == 0), stop=False, is_transpose=True,
                                            skip_group_check=True)
                last.then_inc(res_placed, 1)

            def up(b, t, j):
                p = b % 2
                rows = slice(t * P, (t + 1) * P)
                n = JT * b + j + 1
                if b == B - 1 and t >= 2:
                    n += JT
                if t == 0 or (t == 2 and b == B - 1):
                    pe.wait_ge(hid_hi_done, n)
                    pe.wait_ge(wu_hi_done, b + 1)
                    pe.wait_ge(wu_lo_done[j], b + 1)
                nc.tensor.matmul(y_ps[:, t, :], hid_hi[:, p, j, rows], wu_hi[:, p, j, :],
                                 start=False, stop=False, skip_group_check=True)
                nc.tensor.matmul(y_ps[:, t, :], hid_hi[:, p, j, rows], wu_lo[:, p, j, :],
                                 start=False, stop=False, skip_group_check=True)
                if t == 0 or (t == 2 and b == B - 1):
                    pe.wait_ge(hid_lo_done, n)
                last = nc.tensor.matmul(y_ps[:, t, :], hid_lo[:, p, j, rows], wu_hi[:, p, j, :],
                                        start=False, stop=(j == JT - 1), skip_group_check=True)
                if j == JT - 1:
                    last.then_inc(y_done, 1)

            warm_up()
            for b in range(B - 1):
                if b == 0:
                    down_whole(b, 0)
                else:
                    down(b, 0)
                down(b, 1)
                pe.wait_ge(x_res_done, KT * (b + 1))
                for t in range(TT):
                    place_residual(b, t)
                for t, j in [(0, 0), (1, 0), (0, 1), (1, 1), (2, 0), (2, 1), (3, 0), (3, 1)]:
                    up(b, t, j)
            b = B - 1
            down_half(b, 0, 0)
            down_half(b, 0, 1)
            down_half(b, 1, 0)
            pe.wait_ge(x_res_done, KT * (b + 1))
            place_residual(b, 0)
            place_residual(b, 1)
            up(b, 0, 0)
            up(b, 0, 1)
            down_half(b, 1, 1)
            up(b, 1, 0)
            up(b, 1, 1)
            for t in range(2, TT):
                place_residual(b, t)
                for j in range(JT):
                    up(b, t, j)


def kernel(x, itok_B_1_2, L0_cond_W_down, L0_cond_b_down, L0_cond_W_up, L0_cond_b_up, L0_cond_ln_w, L0_cond_ln_b):
    import numpy as np
    import concourse.bacc as bacc
    from concourse.bass_utils import run_bass_kernel_spmd

    x = np.asarray(x)
    B, S, H = x.shape
    E, _, BN = L0_cond_W_down.shape
    kt, jt, tt = H // P, BN // P, S // P
    by_partition = lambda a, n: np.asarray(a).reshape(E, n, P, -1).transpose(0, 2, 1, 3).reshape(E, P, -1)
    arrays = {
        "x_cols": np.ascontiguousarray(x.reshape(B, P, tt, kt, P).transpose(0, 4, 3, 2, 1).reshape(B, P, kt, S)),
        "expert_of_batch": np.ascontiguousarray(np.asarray(itok_B_1_2).reshape(1, B)),
        "weights": np.concatenate([by_partition(L0_cond_b_down, jt), by_partition(L0_cond_b_up, kt),
                                   by_partition(L0_cond_W_down, kt), by_partition(L0_cond_W_up, jt)], axis=2),
        "ln_rows": np.concatenate([np.asarray(L0_cond_ln_w), np.asarray(L0_cond_ln_b)], axis=1),
    }
    nc = bacc.Bacc("TRN2", target_bir_lowering=False, num_devices=1)
    ins = [nc.dram_tensor(name, a.shape, mybir.dt.from_np(a.dtype), kind="ExternalInput").ap()
           for name, a in arrays.items()]
    out = nc.dram_tensor("out", (B, S, H), F32, kind="ExternalOutput").ap()
    conditional_adapter_kernel(nc, *ins, out)
    r = run_bass_kernel_spmd(nc, [arrays], core_ids=[0])
    return r.results[0]["out"]
```
